# Optimizing a Trainium2 kernel written in Bass

```python
import numpy as np
import jax
import jax.numpy as jnp

def _softmax(x, axis=-1):
    return jax.nn.softmax(x, axis=axis)

def _gelu(x):
    return jax.nn.gelu(x, approximate=True)

def _silu(x):
    return jax.nn.silu(x)

def _sigmoid(x):
    return jax.nn.sigmoid(x)

def _layernorm(x, axis=-1, eps=1e-05):
    m = jnp.mean(x, axis=axis, keepdims=True)
    v = jnp.var(x, axis=axis, keepdims=True)
    return (x - m) / jnp.sqrt(v + eps)

def _scatter_add(tgt, idx, src, axis=0):
    return tgt.at[idx].add(src)

def _segment_sum(src, seg, n):
    return jax.ops.segment_sum(src, seg, n)
kernel_name = 'mk_flamingo_gated_d1_seqx_r8_b656b7'

def setup_inputs(seed: int=0):
    np.random.seed(seed)
    _w = jnp.asarray

    def _rec_inputs():
        import jax
        import jax.numpy as jnp
        _rk = jax.random.key(seed)
        x = -0.000125 + 0.9999 * jax.random.normal(jax.random.fold_in(_rk, 1), (32, 100, 256), jnp.float32)
        _lenS = 100 - jax.random.randint(jax.random.fold_in(_rk, 7), (32,), 0, max(1, 100 // 4) + 1, jnp.int32)
        _lenS2 = 1444 - jax.random.randint(jax.random.fold_in(_rk, 8), (32,), 0, max(1, 1444 // 4) + 1, jnp.int32)
        _ctx_2048P = jax.random.normal(jax.random.fold_in(_rk, 11), (32, 16, 256), jnp.float32)
        _ctx_2048c = jax.random.dirichlet(jax.random.fold_in(_rk, 511), 0.3 * jnp.ones((16,), jnp.float32), (32, 1444))
        _ctx_2048t = jnp.einsum('bsk,bkd->bsd', _ctx_2048c, _ctx_2048P)
        _ctx_2048t = _ctx_2048t * jax.lax.rsqrt(jnp.mean(jnp.square(_ctx_2048t)) + 1e-12) * 0.953939
        ctx_2048 = 4.13588e-05 + 0.999923 * (_ctx_2048t + 0.3 * jax.random.normal(jax.random.fold_in(_rk, 611), (32, 1444, 256), jnp.float32))
        _g = jax.random.normal(jax.random.fold_in(_rk, 9001), (2, 1), jnp.float32)
        _g = jnp.sign(_g) * jnp.maximum(jnp.abs(_g), 1.0) + (_g == 0) * 1.0
        g_xattn = _g[0]
        g_ffn = _g[1]
        return (x, ctx_2048, g_xattn, g_ffn)
    x, ctx_2048, g_xattn, g_ffn = _rec_inputs()

    def _L0_xattn_setup():
        import jax, jax.numpy as jnp
        import numpy as np
        D_MODEL = 256
        NUM_HEADS = 16
        HEAD_DIM = D_MODEL // NUM_HEADS
        key = jax.random.key(seed)
        ks = jax.random.split(key, 10)
        B, S, T = (4, 512, 128)
        s = 1.0 / np.sqrt(D_MODEL)
        inp = {'query': jax.random.normal(ks[0], (B, S, D_MODEL), jnp.float32), 'key_value': jax.random.normal(ks[1], (B, T, D_MODEL), jnp.float32), 'Wq': jax.random.normal(ks[2], (D_MODEL, D_MODEL), jnp.float32) * s, 'bq': jnp.zeros((D_MODEL,), jnp.float32), 'Wk': jax.random.normal(ks[3], (D_MODEL, D_MODEL), jnp.float32) * s, 'bk': jnp.zeros((D_MODEL,), jnp.float32), 'Wv': jax.random.normal(ks[4], (D_MODEL, D_MODEL), jnp.float32) * s, 'bv': jnp.zeros((D_MODEL,), jnp.float32), 'Wo': jax.random.normal(ks[5], (D_MODEL, D_MODEL), jnp.float32) * s, 'bo': jnp.zeros((D_MODEL,), jnp.float32)}
        return inp
    _L0_xattn_all = _L0_xattn_setup()
    _L0_xattn_in = {k: v for k, v in _L0_xattn_all.items() if k in ('Wq', 'bq', 'Wk', 'bk', 'Wv', 'bv', 'Wo', 'bo')}
    del _L0_xattn_all

    def _L0_ffn_setup():
        import jax, jax.numpy as jnp
        import numpy as np
        E, K = (12, 3)
        B, S, H, I = (2, 256, 256, 640)

        def _forward(x, Wr, br, w1, b1, w2, b2, Wp1, bp1, Wp2, bp2):
            logits = jnp.einsum('bsh,he->bse', x, Wr) + br
            probs = jax.nn.softmax(logits, axis=-1)
            top_vals, top_idx = jax.lax.top_k(probs, K)
            ew = jax.nn.softmax(top_vals, axis=-1)
            out = jnp.zeros_like(x)
            for e in range(E):
                sel = top_idx == e
                mask = sel.any(axis=-1)
                cnt = sel.sum()
                w_e = jnp.sum(jnp.where(sel, ew, 0.0)) / jnp.maximum(cnt, 1).astype(ew.dtype)
                h = jax.nn.relu(jnp.einsum('bsh,hi->bsi', x, w1[e]) + b1[e])
                h = jnp.einsum('bsi,ih->bsh', h, w2[e]) + b2[e]
                out = out + mask[..., None].astype(x.dtype) * (w_e * h)
            pooled = out.mean(axis=1)
            phi = jax.nn.sigmoid(jax.nn.relu(pooled @ Wp1 + bp1) @ Wp2 + bp2)
            phi_mask = (phi > 0.7).astype(out.dtype)[:, :, None]
            return out * (1.0 - phi_mask * 0.8)
        key = jax.random.key(seed)
        ks = jax.random.split(key, 8)
        sH = np.float32(1.0 / np.sqrt(H))
        sI = np.float32(1.0 / np.sqrt(I))
        sH2 = np.float32(1.0 / np.sqrt(H // 2))
        return {'hidden_states': jax.random.normal(ks[0], (B, S, H), jnp.float32), 'Wr': jax.random.normal(ks[1], (H, E), jnp.float32) * sH, 'br': jnp.zeros((E,), jnp.float32), 'w1': jax.random.normal(ks[2], (E, H, I), jnp.float32) * sH, 'b1': jnp.zeros((E, I), jnp.float32), 'w2': jax.random.normal(ks[3], (E, I, H), jnp.float32) * sI, 'b2': jnp.zeros((E, H), jnp.float32), 'Wp1': jax.random.normal(ks[4], (H, H // 2), jnp.float32) * sH, 'bp1': jnp.zeros((H // 2,), jnp.float32), 'Wp2': jax.random.normal(ks[5], (H // 2, 1), jnp.float32) * sH2, 'bp2': jnp.zeros((1,), jnp.float32)}
    _L0_ffn_all = _L0_ffn_setup()
    _L0_ffn_in = {k: v for k, v in _L0_ffn_all.items() if k in ('Wr', 'br', 'w1', 'b1', 'w2', 'b2', 'Wp1', 'bp1', 'Wp2', 'bp2')}
    del _L0_ffn_all
    return {'x': x, 'ctx_2048': ctx_2048, 'g_xattn': g_xattn, 'g_ffn': g_ffn, 'L0_xattn_Wq': _L0_xattn_in['Wq'], 'L0_xattn_bq': _L0_xattn_in['bq'], 'L0_xattn_Wk': _L0_xattn_in['Wk'], 'L0_xattn_bk': _L0_xattn_in['bk'], 'L0_xattn_Wv': _L0_xattn_in['Wv'], 'L0_xattn_bv': _L0_xattn_in['bv'], 'L0_xattn_Wo': _L0_xattn_in['Wo'], 'L0_xattn_bo': _L0_xattn_in['bo'], 'L0_ffn_Wr': _L0_ffn_in['Wr'], 'L0_ffn_br': _L0_ffn_in['br'], 'L0_ffn_w1': _L0_ffn_in['w1'], 'L0_ffn_b1': _L0_ffn_in['b1'], 'L0_ffn_w2': _L0_ffn_in['w2'], 'L0_ffn_b2': _L0_ffn_in['b2'], 'L0_ffn_Wp1': _L0_ffn_in['Wp1'], 'L0_ffn_bp1': _L0_ffn_in['bp1'], 'L0_ffn_Wp2': _L0_ffn_in['Wp2'], 'L0_ffn_bp2': _L0_ffn_in['bp2']}

def reference(x, ctx_2048, g_xattn, g_ffn, L0_xattn_Wq, L0_xattn_bq, L0_xattn_Wk, L0_xattn_bk, L0_xattn_Wv, L0_xattn_bv, L0_xattn_Wo, L0_xattn_bo, L0_ffn_Wr, L0_ffn_br, L0_ffn_w1, L0_ffn_b1, L0_ffn_w2, L0_ffn_b2, L0_ffn_Wp1, L0_ffn_bp1, L0_ffn_Wp2, L0_ffn_bp2):
    import jax
    import jax.numpy as jnp

    def _L0_xattn_ref(query, key_value, Wq, bq, Wk, bk, Wv, bv, Wo, bo):
        import jax, jax.numpy as jnp
        import numpy as np
        D_MODEL = 256
        NUM_HEADS = 16
        HEAD_DIM = D_MODEL // NUM_HEADS
        B, S, _ = query.shape
        T = key_value.shape[1]
        Q = query @ Wq.T + bq
        K = key_value @ Wk.T + bk
        V = key_value @ Wv.T + bv
        Q = Q.reshape(B, S, NUM_HEADS, HEAD_DIM).transpose(0, 2, 1, 3)
        K = K.reshape(B, T, NUM_HEADS, HEAD_DIM).transpose(0, 2, 1, 3)
        V = V.reshape(B, T, NUM_HEADS, HEAD_DIM).transpose(0, 2, 1, 3)
        scale = 1.0 / np.sqrt(HEAD_DIM).astype(np.float32)
        scores = jnp.einsum('bhsd,bhtd->bhst', Q, K) * scale
        attn = jax.nn.softmax(scores, axis=-1)
        ctx = jnp.einsum('bhst,bhtd->bhsd', attn, V)
        ctx = ctx.transpose(0, 2, 1, 3).reshape(B, S, D_MODEL)
        return ctx @ Wo.T + bo

    def _L0_ffn_ref(hidden_states, Wr, br, w1, b1, w2, b2, Wp1, bp1, Wp2, bp2):
        import jax, jax.numpy as jnp
        import numpy as np
        E, K = (12, 3)
        B, S, H, I = (2, 256, 256, 640)

        def _forward(x, Wr, br, w1, b1, w2, b2, Wp1, bp1, Wp2, bp2):
            logits = jnp.einsum('bsh,he->bse', x, Wr) + br
            probs = jax.nn.softmax(logits, axis=-1)
            top_vals, top_idx = jax.lax.top_k(probs, K)
            ew = jax.nn.softmax(top_vals, axis=-1)
            out = jnp.zeros_like(x)
            for e in range(E):
                sel = top_idx == e
                mask = sel.any(axis=-1)
                cnt = sel.sum()
                w_e = jnp.sum(jnp.where(sel, ew, 0.0)) / jnp.maximum(cnt, 1).astype(ew.dtype)
                h = jax.nn.relu(jnp.einsum('bsh,hi->bsi', x, w1[e]) + b1[e])
                h = jnp.einsum('bsi,ih->bsh', h, w2[e]) + b2[e]
                out = out + mask[..., None].astype(x.dtype) * (w_e * h)
            pooled = out.mean(axis=1)
            phi = jax.nn.sigmoid(jax.nn.relu(pooled @ Wp1 + bp1) @ Wp2 + bp2)
            phi_mask = (phi > 0.7).astype(out.dtype)[:, :, None]
            return out * (1.0 - phi_mask * 0.8)
        return _forward(hidden_states, Wr, br, w1, b1, w2, b2, Wp1, bp1, Wp2, bp2)
    x = x + jnp.tanh(g_xattn[0]) * _L0_xattn_ref(_layernorm(x, axis=-1), ctx_2048, L0_xattn_Wq, L0_xattn_bq, L0_xattn_Wk, L0_xattn_bk, L0_xattn_Wv, L0_xattn_bv, L0_xattn_Wo, L0_xattn_bo)
    x = x + jnp.tanh(g_ffn[0]) * _L0_ffn_ref(_layernorm(x, axis=-1), L0_ffn_Wr, L0_ffn_br, L0_ffn_w1, L0_ffn_b1, L0_ffn_w2, L0_ffn_b2, L0_ffn_Wp1, L0_ffn_bp1, L0_ffn_Wp2, L0_ffn_bp2)
    return x

_drawn_inputs = setup_inputs


def setup_inputs(seed=0):
    import zlib

    import numpy as np

    out = dict(_drawn_inputs(seed))
    spreads = {'L0_xattn_bq': (0.0, 0.1),
     'L0_xattn_bk': (0.0, 0.1),
     'L0_xattn_bv': (0.0, 0.1),
     'L0_xattn_bo': (0.0, 0.1),
     'L0_ffn_br': (0.0, 0.1),
     'L0_ffn_b1': (0.0, 0.1),
     'L0_ffn_b2': (0.0, 0.1),
     'L0_ffn_bp1': (0.0, 0.1)}
    factors = {}
    for name, (base, spread) in spreads.items():
        noise = np.random.default_rng([zlib.crc32(name.encode()), seed]).standard_normal(out[name].shape)
        drawn = base * np.exp(spread * noise) if base else spread * noise
        out[name] = jnp.asarray(drawn.astype(out[name].dtype))
    for name, factor in factors.items():
        out[name] = (out[name] * factor).astype(out[name].dtype)
    return out
```

```python
import concourse.bass as bass
from concourse import mybir
from contextlib import ExitStack

F32 = mybir.dt.float32
F32R = mybir.dt.float32r
I32 = mybir.dt.int32
U32 = mybir.dt.uint32
ALU = mybir.AluOpType
ACT = mybir.ActivationFunctionType
AX = mybir.AxisListType

B, SQ, D, T = 32, 100, 256, 1444
NH, HD = 16, 16
KD = D // 128
NT = (T + 127) // 128
TW = [min(128, T - 128 * i) for i in range(NT)]
TPC = 4
NC = NT // TPC
CW = [sum(TW[TPC * j:TPC * j + TPC]) for j in range(NC)]
NP = NH // 2
UH = 4
UNITS = NT * NH // UH
MAXES = NC * NH
VW = HD + 1
SCALE = 1.0 / float(HD) ** 0.5
EPS = 1e-5
NE, TOPK, FF = 12, 3, 640
FM = FF // 128
RT = 256
TILES = (B * SQ * TOPK + NE * (RT - 1)) // RT
REGION = B * SQ + RT
XW = D + NE + 1
SLOTS = TOPK * B * SQ
NCMP = (B * SQ + RT - 1) // RT
LAG = 2
RING_S, RING_M, RING_P = 3, 2, 4


def live(n, lag):
    return 0 <= n - lag < B if isinstance(n, int) else True


def wait(eng, sem, value):
    if not isinstance(value, int) or value > 0:
        eng.wait_ge(sem, value)


def maxes_at(w):
    if not 4 <= w < 44:
        return []
    first = sum(2 if u % 5 == 4 else 1 for u in range(4, w))
    return list(range(first, first + (2 if w % 5 == 4 else 1)))


def jobs_at(w):
    fixed = {1: "ut", 5: "at", 9: "o", 13: "xq", 17: "xt", 21: "lg", 25: "qt", 35: "px", 47: "nm"}
    jobs = [(fixed[w], 0)] if w in fixed else []
    if w % 4 == 2 and w >= 6:
        jobs.append(("v", (w - 6) // 4))
    if w in (15, 31, UNITS):
        jobs += [("k", 2 * (w // 16 if w < UNITS else 2)), ("k", 2 * (w // 16 if w < UNITS else 2) + 1)]
    if w == UNITS:
        jobs.append(("v", NT - 1))
    return jobs


ALL_JOBS = [j for w in range(UNITS + 1) for j in jobs_at(w)]
RING_SLOTS = len(ALL_JOBS) + len(ALL_JOBS) % 2
STAGE = {"v": 0, "k": 0, "xq": 0, "qt": 0, "nm": 1, "ut": 3, "at": 3, "o": 3, "xt": 3, "lg": 3, "px": 3}
PER = {k: sum(j[0] == k for j in ALL_JOBS) for k in STAGE}


def before(kind, index, n):
    at, step = ALL_JOBS.index((kind, index)), n
    while True:
        at -= 2
        if at < 0:
            at, step = at + RING_SLOTS, step - 1
        if isinstance(step, int) and step < 0:
            return None
        if at < len(ALL_JOBS) and live(step, STAGE[ALL_JOBS[at][0]]):
            return (*ALL_JOBS[at], step)


def program(nc, x, ctxT, g_xattn, g_ffn, wqT, bq, wkT, bk, wvT, bv, woT, bo, wr, br,
            w1, b1, w2, b2, wp1, bp1, wp2, bp2, out):
    xs = nc.dram_tensor("rows_by_expert", [NE * REGION, XW], F32, kind="Internal").ap()
    ys = nc.dram_tensor("results_by_token", [1 + SLOTS + TILES * RT, D], F32, kind="Internal").ap()
    x1s = nc.dram_tensor("after_attention", [B, SQ, D], F32, kind="Internal").ap()
    with ExitStack() as ctx:
        counts = ctx.enter_context(nc.sbuf_tensor("counts", [SQ, 2 * NE], F32))
        attention(nc, x, ctxT, g_xattn, wqT, bq, wkT, bk, wvT, bv, woT, bo, wr, br,
                  xs, x1s, counts)
        experts(nc, xs, ys, x1s, counts, g_ffn, w1, b1, w2, b2, wp1, bp1, wp2, bp2, out)


def attention(nc, x, ctxT, g_xattn, wqT, bq, wkT, bk, wvT, bv, woT, bo, wr, br,
              xs, x1s, counts):
    with ExitStack() as ctx:
        def sb(name, shape, dt=F32):
            return ctx.enter_context(nc.sbuf_tensor(name, shape, dt))

        def pb(name, shape):
            return ctx.enter_context(nc.psum_tensor(name, shape, F32))

        def sem(name):
            return ctx.enter_context(nc.semaphore(name))

        w_qo = sb("w_qo", [128, 2, KD, D])
        w_hi = sb("w_hi", [128, 2, KD, D], F32R)
        w_lo = sb("w_lo", [128, 2, KD, D], F32R)
        wr_sb = sb("wr_sb", [128, KD, NE])
        br_b = sb("br_b", [SQ, NE])
        bq_c = sb("bq_c", [128, KD])
        bk_c = sb("bk_c", [128, KD])
        bv_c = sb("bv_c", [128, KD])
        bo_b = sb("bo_b", [SQ, D])
        gate_raw = sb("gate_raw", [128, 1])
        gate = sb("gate", [128, 1])
        const_row = sb("const_row", [SQ, D])
        ident = sb("ident", [128, 128])
        tri = sb("tri", [SQ, SQ])
        ones = sb("ones", [SQ, SQ])
        lower = sb("lower", [SQ, NE, NE])
        kth = sb("kth", [SQ, TOPK, NE])
        base = sb("base", [SQ, NE])
        slots_i = sb("slots_i", [SQ, TOPK, NE], I32)
        slots = sb("slots", [SQ, TOPK, NE])
        slot_of = sb("slot_of", [SQ, TOPK, NE])
        half = sb("half", [SQ, 1])
        eps = sb("eps", [SQ, 1])
        zero = sb("zero_col", [128, 1])

        ctx_raw = sb("ctx_raw", [128, KD, T])
        ctx_hi = sb("ctx_hi", [128, KD, T], F32R)
        ctx_lo = sb("ctx_lo", [128, KD, T], F32R)
        k_hi = sb("k_hi", [128, KD, 128 * TPC], F32R)
        k_lo = sb("k_lo", [128, KD, 128 * TPC], F32R)
        k_stack = [sb(f"k_stack{p}", [97, NP, T], F32R) for p in range(2)]
        q_stack = [sb(f"q_stack{p}", [97, NP, 2 * SQ], F32R) for p in range(2)]
        v_ones = [sb(f"v_ones{p}", [128, NT, NH, VW]) for p in range(2)]
        w_kv = v_ones[1][:].rearrange("p t h v -> p (t h v)")[:, 0:2 * KD * D].rearrange(
            "p (i k o) -> p i k o", i=2, k=KD)
        probs = sb("probs", [128, RING_P, UH * SQ])

        x_in = sb("x_in", [SQ, D])
        stats1 = sb("stats1", [SQ, 6])
        mv1 = sb("mv1", [SQ, 2])
        rstd1 = sb("rstd1", [SQ, 2])
        xT_q = sb("xT_q", [128, KD, SQ])
        q_hi = sb("q_hi", [128, KD, SQ], F32R)
        q_lo = sb("q_lo", [128, KD, SQ], F32R)
        max_part = sb("max_part", [SQ, NH, NC])
        neg_max = sb("neg_max", [SQ, NH])
        neg_max_rows = sb("neg_max_rows", [NH, SQ], F32R)

        pv_out = sb("pv_out", [128, 4 * SQ])
        bv_wide = pv_out[:, 0:KD * SQ].rearrange("p (k s) -> p k s", k=KD)
        inv_sum = sb("inv_sum", [SQ, NH])
        heads = sb("heads", [SQ, D])
        headsT = sb("headsT", [128, KD, SQ])
        x_res = sb("x_res", [SQ, D])
        x1 = sb("x1", [SQ, D])
        stats2 = sb("stats2", [SQ, 6])
        mv2 = sb("mv2", [SQ, 2])
        rstd2 = sb("rstd2", [SQ, 2])
        x_row = sb("x_row", [SQ, XW])
        xn = x_row[:, 0:D]
        xnT = sb("xnT", [128, KD, SQ])
        logits = sb("logits", [SQ, NE])
        small = sb("small", [SQ, 16])
        pexp = sb("pexp", [SQ, NE])
        pr = sb("pr", [SQ, NE])
        gt = sb("gt", [SQ, NE, NE])
        eq = sb("eq", [SQ, NE, NE])
        rank = sb("rank", [SQ, NE])
        onehot = sb("onehot", [SQ, TOPK, NE])
        picked = sb("picked", [SQ, TOPK, NE])
        topv = sb("topv", [SQ, TOPK])
        ew = sb("ew", [SQ, TOPK])
        chosen = sb("chosen", [SQ, 2 * NE])
        place = sb("place", [SQ, NE])
        route = sb("route", [SQ, TOPK])
        row_of = sb("row_of", [SQ, TOPK], U32)

        score_ps = [pb(f"score_ps{i}", [128, 512]) for i in range(RING_S)]
        max_ps = [pb(f"max_ps{i}", [128, 512]) for i in range(RING_M)]
        job_ps = [pb(f"job_ps{i}", [128, 512]) for i in range(2)]
        pv_ps = pb("pv_ps", [128, 512])

        weights_in = sem("weights_in")
        const_ready = sem("const_ready")
        split_w = sem("split_w")
        gate_ready = sem("gate_ready")
        const_mm = sem("const_mm")
        setup = sem("setup")
        pool_setup = sem("pool_setup")
        ctx_in = [sem(f"ctx_in{j}") for j in range(NC)]
        ctx_hi_ready = sem("ctx_hi_ready")
        ctx_split = sem("ctx_split")
        done = {k: sem(f"done_{k}") for k in STAGE}
        freed = {k: sem(f"freed_{k}") for k in STAGE}
        k_hi_ready = sem("k_hi_ready")
        q_hi_ready = sem("q_hi_ready")
        k_stacked = [sem(f"k_stacked{j}") for j in range(NC)]
        q_stacked = sem("q_stacked")
        x_loaded = sem("x_loaded")
        res_loaded = sem("res_loaded")
        mv1_ready = sem("mv1_ready")
        rstd1_ready = sem("rstd1_ready")
        xln_ready = sem("xln_ready")
        max_done = sem("max_done")
        max_read = sem("max_read")
        neg_max_ready = sem("neg_max_ready")
        max_row_in = sem("max_row_in")
        score_done = sem("score_done")
        exp_done = sem("exp_done")
        pv_done = sem("pv_done")
        pv_read = sem("pv_read")
        heads_ready = sem("heads_ready")
        xconst_ready = sem("xconst_ready")
        x1_stored = sem("x1_stored")
        mv2_ready = sem("mv2_ready")
        rstd2_ready = sem("rstd2_ready")
        xn_ready = sem("xn_ready")
        logits_ready = sem("logits_ready")
        pexp_ready = sem("pexp_ready")
        topv_ready = sem("topv_ready")
        ew_ready = sem("ew_ready")
        chosen_ready = sem("chosen_ready")
        row_ready = sem("row_ready")
        counted = sem("counted")
        scattered = sem("scattered")
        dve_own = sem("dve_own")
        dve_own_p = sem("dve_own_p")
        pool_own = sem("pool_own")
        always = sem("always")

        N_WEIGHTS, N_CONST = 11, 8 + NE + TOPK
        PEEL, STEADY = 4, 26
        STEPS = B + 3

        def steps(eng, step):
            for n in range(PEEL):
                step(n, n % 2)
            number = eng.alloc_register("step_number")
            eng.reg_mov(number, PEEL)
            with eng.Fori(0, STEADY // 2):
                for par in range(2):
                    step(eng.snap(number, min_val=PEEL + par, max_val=PEEL + STEADY - 2 + par), (PEEL + par) % 2)
                    eng.reg_add(number, number, 1)
            for n in range(PEEL + STEADY, STEPS):
                step(n, n % 2)

        k0 = [128 * TPC * j for j in range(NC)]

        block = ctx.enter_context(nc.Block())

        @block.sync
        def _(sp):
            sp.dma_start(w_kv[:, 0], wkT).then_inc(weights_in, 16)
            sp.dma_start(w_kv[:, 1], wvT).then_inc(weights_in, 16)
            sp.dma_start(ctx_raw[:, :, 0:CW[0]], ctxT[0][:, :, 0:CW[0]]).then_inc(ctx_in[0], 16)
            sp.dma_start(x_in[:], x[0]).then_inc(x_loaded, 16)
            sp.dma_start(w_qo[:, 0], wqT).then_inc(weights_in, 16)
            sp.dma_start(bq_c[:], bq).then_inc(weights_in, 16)
            sp.dma_start(bk_c[:], bk).then_inc(weights_in, 16)
            for j in range(1, NC):
                sp.dma_start(ctx_raw[:, :, k0[j]:k0[j] + CW[j]],
                             ctxT[0][:, :, k0[j]:k0[j] + CW[j]]).then_inc(ctx_in[j], 16)
            sp.dma_start(w_qo[:, 1], woT).then_inc(weights_in, 16)
            sp.dma_start(bv_c[:], bv).then_inc(weights_in, 16)
            sp.dma_start(wr_sb[:], wr).then_inc(weights_in, 16)
            sp.dma_start(bo_b[:], bo.partition_broadcast(SQ)).then_inc(weights_in, 16)
            sp.dma_start(br_b[:], br.partition_broadcast(SQ)).then_inc(weights_in, 16)
            sp.dma_start(gate_raw[:], g_xattn.partition_broadcast(128)).then_inc(weights_in, 16)

            def ready(sem, value):
                wait(sp, sem, value)
                sp.wait_ge(always, 1)

            def step(n, par):
                def stack_keys(j, other):
                    for q in range(4):
                        for part, src in ((0, k_hi), (1, k_hi), (2, k_lo)):
                            sp.dma_start(k_stack[other][32 * part:32 * part + 32, q::4, k0[j]:k0[j] + CW[j]].bitcast(F32),
                                         src[32 * q:32 * q + 32, :, 0:CW[j]].bitcast(F32)).then_inc(k_stacked[j], 16)

                if live(n, 1):
                    ready(freed["qt"], n)
                    ready(score_done, UNITS * (n - 2))
                    for q in range(4):
                        for e in range(2):
                            for part, src in ((0, q_hi), (1, q_lo), (2, q_hi)):
                                sp.dma_start(
                                    q_stack[1 - par][32 * part + HD * e:32 * part + HD * e + HD, q::4,
                                                     SQ * e:SQ * e + SQ].bitcast(F32),
                                    src[32 * q + HD * e:32 * q + HD * e + HD, :, :].bitcast(F32)).then_inc(q_stacked, 16)
                    ready(freed["k"], 2 * NC * n)
                    stack_keys(NC - 1, 1 - par)
                if live(n, 3):
                    ready(freed["o"], n - 3)
                    sp.dma_start(x_res[:], x[n - 3]).then_inc(res_loaded, 16)
                if live(n + 1, 0):
                    ready(ctx_split, NC * n + 1)
                    sp.dma_start(ctx_raw[:, :, 0:CW[0]], ctxT[n + 1][:, :, 0:CW[0]]).then_inc(ctx_in[0], 16)
                    ready(done["xq"], n + 1)
                    sp.dma_start(x_in[:], x[n + 1]).then_inc(x_loaded, 16)
                if live(n, 3):
                    ready(freed["o"], n - 2)
                    sp.dma_start(x1s[n - 3], x1[:]).then_inc(x1_stored, 16)
                for j in range(NC - 1):
                    if live(n, 0):
                        ready(freed["k"], 2 * NC * n + 2 * j + 2)
                        ready(score_done, TPC * UH * (NC * (n - 2) + j + 1))
                        stack_keys(j, par)
                    if live(n + 1, 0):
                        ready(ctx_split, NC * n + j + 2)
                        sp.dma_start(ctx_raw[:, :, k0[j + 1]:k0[j + 1] + CW[j + 1]],
                                     ctxT[n + 1][:, :, k0[j + 1]:k0[j + 1] + CW[j + 1]]).then_inc(ctx_in[j + 1], 16)
                if live(n, 1):
                    ready(freed["nm"], n)
                    sp.dma_start(q_stack[1 - par][96:97, :, :].rearrange("p j c -> p (j c)").bitcast(F32),
                                 neg_max_rows[:].bitcast(F32)).then_inc(max_row_in, 16)

            steps(sp, step)
            sp.wait_ge(x1_stored, 16 * B)

        @block.gpsimd
        def _(pool):
            pool.memset(ones[:], 1.0).then_inc(always, 1)
            pool.memset(ident[:], 0.0).then_inc(pool_setup, 1)
            pool.memset(tri[:], 1.0).then_inc(pool_setup, 1)
            pool.memset(lower[:], 1.0).then_inc(pool_setup, 1)
            pool.memset(half[:], -0.5).then_inc(const_ready, 1)
            pool.memset(eps[:], EPS).then_inc(const_ready, 1)
            pool.memset(zero[:], 0.0).then_inc(const_ready, 1)
            pool.wait_ge(pool_setup, 3)
            pool.affine_select(out=ident[:], in_=ident[:], compare_op=ALU.not_equal, fill=1.0, base=0,
                               pattern=[[-1, 128]], channel_multiplier=1).then_inc(const_ready, 1)
            pool.affine_select(out=tri[:], in_=tri[:], compare_op=ALU.is_gt, fill=0.0, base=0,
                               pattern=[[1, SQ]], channel_multiplier=-1).then_inc(const_ready, 1)
            pool.affine_select(out=lower[:], in_=lower[:], compare_op=ALU.is_gt, fill=0.0, base=0,
                               pattern=[[1, NE], [-1, NE]], channel_multiplier=0).then_inc(const_ready, 1)
            for e in range(NE):
                pool.memset(base[:, e:e + 1], float(e * REGION)).then_inc(const_ready, 1)
            for k in range(TOPK):
                pool.memset(kth[:, k, :], float(k)).then_inc(const_ready, 1)
            pool.iota(slots_i[:], pattern=[[B * SQ, TOPK], [0, NE]], base=1,
                      channel_multiplier=1).then_inc(const_ready, 1)
            pool.memset(counts[:], 0.0).then_inc(const_ready, 1)
            pool.wait_ge(const_ready, N_CONST)

            def split(b, j):
                wait(pool, ctx_in[j], 16 * (b + 1))
                wait(pool, done["v"], NT * (b - 1) + TPC * (j + 1))
                a = (slice(None), slice(None), slice(k0[j], k0[j] + CW[j]))
                pool.tensor_tensor(ctx_hi[a], ctx_raw[a], zero[:].unsqueeze(2).broadcast_to([128, KD, CW[j]]),
                                   ALU.add).then_inc(ctx_hi_ready, 1)
                wait(pool, ctx_hi_ready, NC * b + j + 1)
                pool.tensor_tensor(ctx_lo[a], ctx_raw[a], ctx_hi[a].bitcast(F32),
                                   ALU.subtract).then_inc(ctx_split, 1)

            def inv_std(own, mv, rstd, ready, mv_ready, b):
                wait(pool, mv_ready, b + 1)
                pool.tensor_tensor(rstd[:, 1:2], mv[:, 1:2], eps[:], ALU.add).then_inc(pool_own, 1)
                wait(pool, pool_own, own)
                pool.tensor_tensor(rstd[:, 0:1], rstd[:, 1:2], half[:], ALU.pow).then_inc(ready, 1)

            split(0, 0)

            def step(n, par):
                p_on, e_on = live(n, 0), live(n, 3)
                b3 = n - 3
                own = (min(n, B) if isinstance(n, int) else n) + (max(b3, 0) if isinstance(n, int) else b3)
                if p_on:
                    inv_std(own + 1, mv1, rstd1, rstd1_ready, mv1_ready, n)
                    split(n, 1)
                if e_on:
                    wait(pool, res_loaded, 16 * (b3 + 1))
                    pool.tensor_tensor(x_res[:], x_res[:], const_row[:], ALU.add).then_inc(xconst_ready, 1)
                    inv_std(own + (2 if p_on else 1), mv2, rstd2, rstd2_ready, mv2_ready, b3)
                if p_on:
                    split(n, 2)
                if live(n + 1, 0):
                    split(n + 1, 0)
                if e_on:
                    wait(pool, row_ready, b3 + 1)
                    pool.tensor_tensor(counts[:], counts[:], chosen[:], ALU.add).then_inc(counted, 1)
                    for k in range(TOPK):
                        pool.indirect_dma_start(
                            out=xs, out_offset=bass.IndirectOffsetOnAxis(ap=row_of[:, k:k + 1], axis=0),
                            in_=x_row[:], in_offset=None).then_inc(scattered, 16)

            pool.wait_ge(const_mm, 2)
            steps(pool, step)
            pool.wait_ge(scattered, 16 * TOPK * B)

        @block.scalar
        def _(act):
            act.wait_ge(weights_in, 16 * N_WEIGHTS)
            act.activation(gate[:], gate_raw[:], ACT.Tanh).then_inc(gate_ready, 1)

            def evacuate(kind, index, n):
                b, bank = n - STAGE[kind], job_ps[ALL_JOBS.index((kind, index)) % 2]
                if kind == "v":
                    wait(act, done["v"], NT * b + index + 1)
                    act.activation(v_ones[b_par(n)][0:TW[index], index, :, 0:HD],
                                   bank[0:TW[index], 0:D].rearrange("p (h d) -> p h d", h=NH),
                                   ACT.Copy).then_inc(freed["v"], 1)
                if kind == "k":
                    j, o = index // 2, index % 2
                    wait(act, done["k"], 2 * NC * b + index + 1)
                    if o == 0:
                        j_last = (j - 1) % NC
                        wait(act, k_stacked[j_last], 16 * 12 * (b + 1 if j else b))
                    act.activation(k_hi[:, o, 0:CW[j]], bank[:, 0:CW[j]], ACT.Identity,
                                   bias=bk_c[:, o:o + 1]).then_inc(k_hi_ready, 1)
                if kind == "xq":
                    wait(act, done["xq"], b + 1)
                    act.activation(xT_q[:].rearrange("p k s -> p (k s)"), bank[:, 0:KD * SQ],
                                   ACT.Copy).then_inc(freed["xq"], 1)
                if kind == "qt":
                    wait(act, done["qt"], b + 1)
                    wait(act, q_stacked, 16 * 24 * b)
                    for o in range(KD):
                        act.activation(q_hi[:, o, :], bank[:, o * SQ:o * SQ + SQ], ACT.Identity,
                                       bias=bq_c[:, o:o + 1]).then_inc(q_hi_ready, 1)
                if kind == "nm":
                    wait(act, done["nm"], b + 1)
                    wait(act, max_row_in, 16 * b)
                    act.activation(neg_max_rows[:], bank[0:NH, 0:SQ], ACT.Copy).then_inc(freed["nm"], 1)
                if kind == "at":
                    wait(act, done["at"], b + 1)
                    act.activation(headsT[:].rearrange("p k s -> p (k s)"), bank[:, 0:KD * SQ],
                                   ACT.Copy).then_inc(freed["at"], 1)
                if kind == "xt":
                    wait(act, done["xt"], b + 1)
                    act.activation(xnT[:].rearrange("p k s -> p (k s)"), bank[:, 0:KD * SQ],
                                   ACT.Copy).then_inc(freed["xt"], 1)

            def b_par(n):
                return step_par[0]

            step_par = [0]

            def step(n, par):
                step_par[0] = par
                b2, b3 = n - 2, n - 3
                for w in range(UNITS + 1):
                    if w == 0 and live(n, 3):
                        wait(act, pv_done, UNITS * (b3 + 1))
                        act.activation(pv_out[:], pv_ps[:, 0:4 * SQ], ACT.Copy).then_inc(pv_read, 1)
                    if w < UNITS and live(n, 2):
                        tw = TW[w // UH]
                        wait(act, score_done, UNITS * b2 + w + 1)
                        wait(act, pv_done, UNITS * b2 + w + 1 - RING_P)
                        act.activation(probs[0:tw, w % RING_P, :], score_ps[w % RING_S][0:tw, 0:UH * SQ],
                                       ACT.Exp, scale=SCALE).then_inc(exp_done, 1)
                    for kind, index in jobs_at(w):
                        if live(n, STAGE[kind]):
                            evacuate(kind, index, n)
                    if w == 24 and live(n, 3):
                        wait(act, logits_ready, b3 + 1)
                        act.activation(pexp[:], logits[:], ACT.Exp, bias=small[:, 0:1],
                                       accum_out=small[:, 1:2]).then_inc(pexp_ready, 1)
                    if w == 36 and live(n, 3):
                        wait(act, topv_ready, b3 + 1)
                        act.activation(ew[:], topv[:], ACT.Exp, bias=small[:, 3:4],
                                       accum_out=small[:, 4:5]).then_inc(ew_ready, 1)

            steps(act, step)

        @block.vector
        def _(dve):
            own = [0]

            def link(ins):
                own[0] += 1
                ins.then_inc(setup, 1)
                dve.wait_ge(setup, own[0])

            link(dve.memset(pv_ps[:], 0.0))
            for p in range(2):
                link(dve.memset(q_stack[p][:].bitcast(F32), 0.0))
                link(dve.memset(k_stack[p][96:97, :, :].bitcast(F32), 1.0))
            dve.wait_ge(weights_in, 16 * N_WEIGHTS)
            for i in range(2):
                link(dve.tensor_copy(w_hi[:, i], w_kv[:, i]))
                link(dve.tensor_tensor(w_lo[:, i], w_kv[:, i], w_hi[:, i].bitcast(F32), ALU.subtract))
            for k in range(KD):
                link(dve.tensor_copy(bv_wide[:, k, :], bv_c[:, k:k + 1].broadcast_to([128, SQ])))
            for p in range(2):
                link(dve.memset(v_ones[p][:, :, :, HD:VW], 1.0))
                link(dve.memset(v_ones[p][:, NT - 1], 0.0))
                link(dve.memset(v_ones[p][0:TW[NT - 1], NT - 1, :, HD:VW], 1.0))
            dve.memset(small[:], 0.0).then_inc(split_w, 1)
            dve.wait_ge(gate_ready, 1)
            dve.wait_ge(const_mm, 1)
            link(dve.tensor_tensor(const_row[:], job_ps[0][0:SQ, 0:D], bo_b[:], ALU.add))
            dve.tensor_scalar(const_row[:], const_row[:], gate[0:SQ], None, ALU.mult).then_inc(const_mm, 1)
            dve.wait_ge(const_ready, N_CONST)
            link(dve.memset(x_row[:], 0.0))
            link(dve.tensor_copy(slots[:], slots_i[:]))

            E_LINKS = 19

            def step(n, par):
                b1_, b3 = n - 1, n - 3
                chain = [0]

                def linked(ins):
                    chain[0] += 1
                    ins.then_inc(dve_own, 1)
                    wait(dve, dve_own, E_LINKS * b3 + chain[0])

                for w in range(UNITS + 1):
                    if live(n, 1):
                        for m in maxes_at(w):
                            j, h = m // NH, m % NH
                            wait(dve, max_done, MAXES * b1_ + m + 1)
                            dve.tensor_reduce(max_part[:, h, j:j + 1], max_ps[m % RING_M][0:SQ, 0:CW[j]], AX.X,
                                              ALU.max).then_inc(max_read, 1)
                        if w == 44:
                            wait(dve, max_read, MAXES * (b1_ + 1))
                            wait(dve, done["nm"], b1_)
                            dve.tensor_reduce(neg_max[:], max_part[:], AX.X, ALU.max,
                                              negate=True).then_inc(neg_max_ready, 1)
                    for kind, index in jobs_at(w):
                        if not live(n, STAGE[kind]):
                            continue
                        b, bank = n - STAGE[kind], job_ps[ALL_JOBS.index((kind, index)) % 2]
                        if kind == "k":
                            j, o = index // 2, index % 2
                            wait(dve, k_hi_ready, 2 * NC * b + index + 1)
                            dve.scalar_tensor_tensor(k_lo[:, o, 0:CW[j]], bank[:, 0:CW[j]], bk_c[:, o:o + 1],
                                                     k_hi[:, o, 0:CW[j]].bitcast(F32), ALU.add,
                                                     ALU.subtract).then_inc(freed["k"], 1)
                        if kind == "qt":
                            wait(dve, q_hi_ready, KD * (b + 1))
                            for o in range(KD):
                                ins = dve.scalar_tensor_tensor(
                                    q_lo[:, o, :], bank[:, o * SQ:o * SQ + SQ], bq_c[:, o:o + 1],
                                    q_hi[:, o, :].bitcast(F32), ALU.add, ALU.subtract)
                            ins.then_inc(freed["qt"], 1)
                        if kind == "o":
                            wait(dve, done["o"], b + 1)
                            wait(dve, xconst_ready, b + 1)
                            wait(dve, x1_stored, 16 * b)
                            dve.scalar_tensor_tensor(x1[:], bank[0:SQ, 0:D], gate[0:SQ], x_res[:],
                                                     ALU.mult, ALU.add).then_inc(freed["o"], 1)
                    if live(n, 0):
                        if w == 0:
                            wait(dve, x_loaded, 16 * (n + 1))
                            dve.bn_stats(stats1[:], x_in[:]).then_inc(dve_own_p, 1)
                        if w == 2:
                            wait(dve, dve_own_p, n + 1)
                        if w == 4:
                            dve.bn_aggr(mv1[:], stats1[:]).then_inc(mv1_ready, 1)
                        if w == 8:
                            wait(dve, rstd1_ready, n + 1)
                            wait(dve, mv1_ready, n + 1)
                            dve.tensor_scalar(x_in[:], x_in[:], mv1[:, 0:1], rstd1[:, 0:1], ALU.subtract,
                                              ALU.mult).then_inc(xln_ready, 1)
                    if live(n, 3):
                        if w == 3:
                            wait(dve, done["ut"], b3 + 1)
                            u = job_ps[ALL_JOBS.index(("ut", 0)) % 2][0:SQ, :].rearrange("p (h c) -> p h c", h=NH)
                            linked(dve.reciprocal(inv_sum[:].unsqueeze(2), u[:, :, HD:VW]))
                            dve.tensor_tensor(heads[:].rearrange("p (h d) -> p h d", h=NH), u[:, :, 0:HD],
                                              inv_sum[:].unsqueeze(2).broadcast_to([SQ, NH, HD]),
                                              ALU.mult).then_inc(freed["ut"], 1)
                        if w == 10:
                            wait(dve, freed["o"], b3 + 1)
                            linked(dve.bn_stats(stats2[:], x1[:]))
                        if w == 11:
                            dve.bn_aggr(mv2[:], stats2[:]).then_inc(mv2_ready, 1)
                        if w == 15:
                            wait(dve, rstd2_ready, b3 + 1)
                            wait(dve, mv2_ready, b3 + 1)
                            wait(dve, scattered, 16 * TOPK * b3)
                            dve.tensor_scalar(xn, x1[:], mv2[:, 0:1], rstd2[:, 0:1], ALU.subtract,
                                              ALU.mult).then_inc(xn_ready, 1)
                        if w == 22:
                            wait(dve, done["lg"], b3 + 1)
                            lg = job_ps[ALL_JOBS.index(("lg", 0)) % 2]
                            dve.tensor_tensor(logits[:], lg[0:SQ, 0:NE], br_b[:], ALU.add).then_inc(freed["lg"], 1)
                        if w == 23:
                            wait(dve, freed["lg"], b3 + 1)
                            dve.tensor_reduce(small[:, 0:1], logits[:], AX.X, ALU.max,
                                              negate=True).then_inc(logits_ready, 1)
                        if w == 26:
                            wait(dve, pexp_ready, b3 + 1)
                            linked(dve.reciprocal(small[:, 2:3], small[:, 1:2]))
                            linked(dve.tensor_scalar(pr[:], pexp[:], small[:, 2:3], None, ALU.mult))
                        p_other = pr[:].unsqueeze(1).broadcast_to([SQ, NE, NE])
                        p_self = pr[:].unsqueeze(2).broadcast_to([SQ, NE, NE])
                        if w == 27:
                            dve.tensor_tensor(gt[:], p_other, p_self, ALU.is_gt)
                            linked(dve.tensor_tensor(eq[:], p_other, p_self, ALU.is_equal))
                        if w == 28:
                            linked(dve.tensor_tensor(eq[:], eq[:], lower[:], ALU.mult))
                        if w == 29:
                            linked(dve.tensor_tensor(gt[:], gt[:], eq[:], ALU.add))
                        if w == 30:
                            linked(dve.tensor_reduce(rank[:], gt[:], AX.X, ALU.add))
                        if w == 31:
                            linked(dve.tensor_tensor(onehot[:], rank[:].unsqueeze(1).broadcast_to([SQ, TOPK, NE]),
                                                     kth[:], ALU.is_equal))
                        if w == 32:
                            wait(dve, counted, b3)
                            linked(dve.tensor_reduce(chosen[:, 0:NE], onehot[:].rearrange("p k e -> p e k"),
                                                     AX.X, ALU.add))
                            dve.tensor_tensor(picked[:], onehot[:], pr[:].unsqueeze(1).broadcast_to(
                                [SQ, TOPK, NE]), ALU.mult).then_inc(chosen_ready, 1)
                        if w == 33:
                            wait(dve, chosen_ready, b3 + 1)
                            linked(dve.tensor_reduce(topv[:], picked[:], AX.X, ALU.add))
                            dve.tensor_scalar(small[:, 3:4], topv[:, 0:1], -1.0, None,
                                              ALU.mult).then_inc(topv_ready, 1)
                        if w == 34:
                            wait(dve, topv_ready, b3 + 1)
                            linked(dve.tensor_tensor(slot_of[:], onehot[:], slots[:], ALU.mult))
                        if w == 35:
                            linked(dve.tensor_reduce(x_row[:, D:D + NE], slot_of[:].rearrange("p k e -> p e k"),
                                                     AX.X, ALU.add))
                            linked(dve.tensor_scalar(slots[:], slots[:], float(SQ), None, ALU.add))
                        if w == 38:
                            wait(dve, ew_ready, b3 + 1)
                            linked(dve.reciprocal(small[:, 5:6], small[:, 4:5]))
                            linked(dve.tensor_scalar(ew[:], ew[:], small[:, 5:6], None, ALU.mult))
                        if w == 39:
                            linked(dve.tensor_tensor(picked[:], onehot[:], ew[:].unsqueeze(2).broadcast_to(
                                [SQ, TOPK, NE]), ALU.mult))
                        if w == 40:
                            dve.tensor_reduce(chosen[:, NE:2 * NE], picked[:].rearrange("p k e -> p e k"),
                                              AX.X, ALU.add)
                            wait(dve, done["px"], b3 + 1)
                            px = job_ps[ALL_JOBS.index(("px", 0)) % 2]
                            dve.tensor_tensor(place[:], px[0:SQ, 0:NE], base[:], ALU.add).then_inc(freed["px"], 1)
                        if w == 41:
                            wait(dve, freed["px"], b3 + 1)
                            linked(dve.tensor_tensor(picked[:], onehot[:], place[:].unsqueeze(1).broadcast_to(
                                [SQ, TOPK, NE]), ALU.mult))
                        if w == 42:
                            linked(dve.tensor_reduce(route[:], picked[:], AX.X, ALU.add))
                            dve.tensor_copy(row_of[:], route[:]).then_inc(row_ready, 1)
                if live(n, 3):
                    assert chain[0] == E_LINKS, chain[0]

            steps(dve, step)

        @block.tensor
        def _(pe):
            pe.wait_ge(split_w, 1)
            for k in range(KD):
                last = pe.matmul(job_ps[0][0:SQ, 0:D], bv_wide[:, k, :], w_qo[:, 1, k, :],
                                 start=(k == 0), stop=(k == KD - 1))
            last.then_inc(const_mm, 1)
            pe.wait_ge(const_ready, N_CONST)
            pe.wait_ge(const_mm, 2)

            def job(kind, index, n, par):
                b, at = n - STAGE[kind], ALL_JOBS.index((kind, index))
                bank = job_ps[at % 2]
                last = before(kind, index, n)
                if last:
                    kind_, index_, n_ = last
                    wait(pe, freed[kind_], PER[kind_] * (n_ - STAGE[kind_]) + index_ + 1)
                if kind == "k":
                    j, o = index // 2, index % 2
                    wait(pe, ctx_split, NC * b + j + 1)
                    keys = slice(k0[j], k0[j] + CW[j])
                    for k in range(KD):
                        for p, (w, c) in enumerate(((w_hi, ctx_hi), (w_hi, ctx_lo), (w_lo, ctx_hi))):
                            ins = pe.matmul(bank[:, 0:CW[j]], w[:, 0, k, 128 * o:128 * o + 128], c[:, k, keys],
                                            start=(k == 0 and p == 0), stop=(k == KD - 1 and p == 2))
                if kind == "v":
                    tw, keys = TW[index], slice(128 * index, 128 * index + TW[index])
                    wait(pe, ctx_split, NC * b + index // TPC + 1)
                    for k in range(KD):
                        for p, (w, c) in enumerate(((w_hi, ctx_hi), (w_lo, ctx_hi), (w_hi, ctx_lo))):
                            ins = pe.matmul(bank[0:tw, 0:D], c[:, k, keys], w[:, 1, k, :],
                                            start=(k == 0 and p == 0), stop=(k == KD - 1 and p == 2))
                if kind == "xq":
                    wait(pe, xln_ready, b + 1)
                    for k in range(KD):
                        ins = pe.transpose(bank[:, k * SQ:k * SQ + SQ], x_in[:, 128 * k:128 * k + 128],
                                           ident[0:SQ, 0:SQ])
                if kind == "qt":
                    wait(pe, freed["xq"], b + 1)
                    for o in range(KD):
                        for k in range(KD):
                            ins = pe.matmul(bank[:, o * SQ:o * SQ + SQ], w_qo[:, 0, k, 128 * o:128 * o + 128],
                                            xT_q[:, k, :], start=(k == 0), stop=(k == KD - 1))
                if kind == "nm":
                    wait(pe, neg_max_ready, b + 1)
                    ins = pe.transpose(bank[0:NH, 0:SQ], neg_max[:], ident[0:SQ, 0:SQ])
                if kind == "ut":
                    wait(pe, pv_read, b + 1)
                    for u in range(4):
                        ins = pe.transpose(bank[0:SQ, 128 * u:128 * u + 128], pv_out[:, u * SQ:u * SQ + SQ],
                                           ident[:])
                if kind == "at":
                    wait(pe, freed["ut"], b + 1)
                    for k in range(KD):
                        ins = pe.transpose(bank[:, k * SQ:k * SQ + SQ], heads[:, 128 * k:128 * k + 128],
                                           ident[0:SQ, 0:SQ])
                if kind == "o":
                    wait(pe, freed["at"], b + 1)
                    for k in range(KD):
                        ins = pe.matmul(bank[0:SQ, 0:D], headsT[:, k, :], w_qo[:, 1, k, :],
                                        start=(k == 0), stop=(k == KD - 1))
                if kind == "xt":
                    wait(pe, xn_ready, b + 1)
                    for k in range(KD):
                        ins = pe.transpose(bank[:, k * SQ:k * SQ + SQ], xn[:, 128 * k:128 * k + 128],
                                           ident[0:SQ, 0:SQ])
                if kind == "lg":
                    wait(pe, freed["xt"], b + 1)
                    for k in range(KD):
                        ins = pe.matmul(bank[0:SQ, 0:NE], xnT[:, k, :], wr_sb[:, k, :],
                                        start=(k == 0), stop=(k == KD - 1))
                if kind == "px":
                    wait(pe, chosen_ready, b + 1)
                    wait(pe, counted, b)
                    pe.matmul(bank[0:SQ, 0:NE], tri[:], chosen[:, 0:NE], start=True, stop=False)
                    ins = pe.matmul(bank[0:SQ, 0:NE], ones[:], counts[:, 0:NE], start=False, stop=True)
                ins.then_inc(done[kind], 1)

            def times_v(w, n, par):
                b2, i, u = n - 2, w // UH, w % UH
                wait(pe, exp_done, UNITS * b2 + w + 1)
                if w == 0:
                    wait(pe, freed["v"], NT * (b2 + 1))
                    wait(pe, pv_read, b2)
                for g in range(UH):
                    ins = pe.matmul(pv_ps[32 * g:32 * g + VW, u * SQ:u * SQ + SQ],
                                    v_ones[par][:, i, UH * u + g, :],
                                    probs[:, w % RING_P, g * SQ:g * SQ + SQ],
                                    start=(w == 0), stop=(i == NT - 1), skip_group_check=True)
                ins.then_inc(pv_done, 1)

            def step(n, par):
                b1_, b2 = n - 1, n - 2
                for w in range(UNITS + LAG):
                    if w < UNITS and live(n, 2):
                        i, u = w // UH, w % UH
                        if w == 0:
                            wait(pe, max_row_in, 16 * (b2 + 1))
                        wait(pe, exp_done, UNITS * b2 + w + 1 - RING_S)
                        for p in range(2):
                            ins = pe.matmul(score_ps[w % RING_S][0:TW[i], 2 * SQ * p:2 * SQ * (p + 1)],
                                            k_stack[par][:, 2 * u + p, 128 * i:128 * i + TW[i]],
                                            q_stack[par][:, 2 * u + p, :], start=True, stop=True)
                        ins.then_inc(score_done, 1)
                    if w < UNITS and live(n, 1):
                        for m in maxes_at(w):
                            j, h = m // NH, m % NH
                            if m == 0:
                                wait(pe, q_stacked, 16 * 24 * (b1_ + 1))
                            if h == 0:
                                wait(pe, k_stacked[j], 16 * 12 * (b1_ + 1))
                            wait(pe, max_read, MAXES * b1_ + m + 1 - RING_M)
                            pe.matmul(max_ps[m % RING_M][0:SQ, 0:CW[j]],
                                      q_stack[1 - par][0:96, h // 2, SQ * (h % 2):SQ * (h % 2) + SQ],
                                      k_stack[1 - par][0:96, h // 2, k0[j]:k0[j] + CW[j]],
                                      start=True, stop=True).then_inc(max_done, 1)
                    if w >= LAG and live(n, 2):
                        times_v(w - LAG, n, par)
                    if w < UNITS:
                        for kind, index in jobs_at(w):
                            if live(n, STAGE[kind]):
                                job(kind, index, n, par)
                for kind, index in jobs_at(UNITS):
                    if live(n, STAGE[kind]):
                        job(kind, index, n, par)

            steps(pe, step)


def experts(nc, xs, ys, x1s, counts, g_ffn, w1, b1, w2, b2, wp1, bp1, wp2, bp2, out):
    with ExitStack() as ctx:
        expert_tiles(nc, xs, ys, counts, w1, b1, w2, b2)
        combine(nc, ys, x1s, g_ffn, wp1, bp1, wp2, bp2, out)


def expert_tiles(nc, xs, ys, counts, w1, b1, w2, b2):
    with ExitStack() as ctx:
        def sb(name, shape, dt=F32):
            return ctx.enter_context(nc.sbuf_tensor(name, shape, dt))

        def pb(name, shape):
            return ctx.enter_context(nc.psum_tensor(name, shape, F32))

        def sem(name):
            return ctx.enter_context(nc.semaphore(name))

        RB = RT // 128
        ident = sb("ident2", [128, 128])
        ones = sb("ones2", [SQ, 128])
        tile_no_i = sb("tile_no_i", [128, TILES], I32)
        tile_no = sb("tile_no", [128, TILES])
        full_i = sb("full_i", [128, NCMP], I32)
        full = sb("full", [128, NCMP])
        first_i = sb("first_i", [128, NE], I32)
        first = sb("first", [128, NE])
        zero = sb("zero", [128, RB, XW])
        spare_i = sb("spare_i", [128, TILES * RB], I32)
        spare = sb("spare", [128, TILES * RB])
        wexp = sb("wexp", [128, NE + 1])
        totals = sb("totals", [128, 2 * NE])
        tmp = sb("tmp", [128, NE])
        more = sb("more", [128, NE, NCMP])
        ntiles = sb("ntiles", [128, NE])
        ends = sb("ends", [128, NE])
        zeros_e = sb("zeros_e", [128, NE])
        past = sb("past", [128, TILES, NE])
        skipped = sb("skipped", [128, TILES, NE])
        t_exp = sb("t_exp", [128, TILES])
        t_before = sb("t_before", [128, TILES])
        t_valid = sb("t_valid", [128, TILES])
        t_row = sb("t_row", [128, TILES])
        pad = sb("pad", [128, NE])
        table = sb("table", [128, 3 * TILES + NE], I32)

        x_t = [sb(f"x_t{p}", [128, RB, XW]) for p in range(2)]
        w1_raw = [sb(f"w1_raw{p}", [128, KD, FF]) for p in range(2)]
        w2_raw = [sb(f"w2_raw{p}", [128, FM, D]) for p in range(2)]
        w1_hi = [sb(f"w1_hi{p}", [128, KD, FF], F32R) for p in range(2)]
        w1_lo = [sb(f"w1_lo{p}", [128, KD, FF], F32R) for p in range(2)]
        w2_hi = [sb(f"w2_hi{p}", [128, FM, D], F32R) for p in range(2)]
        w2_lo = [sb(f"w2_lo{p}", [128, FM, D], F32R) for p in range(2)]
        b1_c = [sb(f"b1_c{p}", [128, FM]) for p in range(2)]
        b2_b = [sb(f"b2_b{p}", [128, D]) for p in range(2)]
        xT_hi = sb("xT_hi", [128, KD, RT], F32R)
        xT_lo = sb("xT_lo", [128, KD, RT], F32R)
        h_raw = [sb(f"h_raw{p}", [128, FM, RT]) for p in range(2)]
        h_hi = [sb(f"h_hi{p}", [128, FM, RT], F32R) for p in range(2)]
        h_lo = [sb(f"h_lo{p}", [128, FM, RT], F32R) for p in range(2)]
        y_t = [sb(f"y_t{p}", [128, RB, D]) for p in range(2)]
        b2_w = [sb(f"b2_w{p}", [128, D]) for p in range(2)]
        no_slot = sb("no_slot", [128, RB])
        slot = [sb(f"slot{p}", [128, RB], U32) for p in range(2)]

        xT_ps = pb("xT_ps", [128, KD * RT])
        h_ps = [pb(f"h_ps{c}", [128, 512]) for c in range(FM)]
        y_ps = [pb(f"y_ps{r}", [128, 512]) for r in range(RB)]

        consts = sem("consts")
        own = sem("own2")
        totals_done = sem("totals_done")
        table_ready = sem("table_ready")
        cleared = sem("cleared")
        x_in = [sem(f"x_in{p}") for p in range(2)]
        w1_in = [sem(f"w1_in{p}") for p in range(2)]
        w2_in = [sem(f"w2_in{p}") for p in range(2)]
        b1_in = [sem(f"b1_in{p}") for p in range(2)]
        b2_in = [sem(f"b2_in{p}") for p in range(2)]
        w1_hi_ready = sem("w1_hi_ready")
        w1_split = sem("w1_split")
        w2_hi_ready = sem("w2_hi_ready")
        w2_split = sem("w2_split")
        xT_done = sem("xT_done")
        xT_hi_ready = sem("xT_hi_ready")
        xT_split = sem("xT_split")
        h_done = sem("h_done")
        h_relu = sem("h_relu")
        h_hi_ready = sem("h_hi_ready")
        h_split = sem("h_split")
        slot_ready = sem("slot_ready")
        no_slot_ready = sem("no_slot_ready")
        b2_w_ready = sem("b2_w_ready")
        y_done = sem("y_done")
        y_read = sem("y_read")
        y_stored = [sem(f"y_stored{p}") for p in range(2)]
        always = sem("always2")

        PEEL = 4
        STEADY = (TILES - 2 - PEEL) // 2 * 2

        def turns(eng, turn):
            for t in range(PEEL):
                turn(t, t % 2, t // 2)
            with eng.Fori(0, STEADY // 2) as it:
                turn(2 * it + PEEL, 0, it + PEEL // 2)
                turn(2 * it + (PEEL + 1), 1, it + PEEL // 2)
            for t in range(PEEL + STEADY, TILES + 1):
                turn(t, t % 2, t // 2)

        def on(t):
            return 0 <= t < TILES if isinstance(t, int) else True

        def nth(s, par, d=0):
            return s + (par + d) // 2 + 1

        block = ctx.enter_context(nc.Block())

        @block.gpsimd
        def _(pool):
            pool.memset(ident[:], 0.0).then_inc(own, 1)
            pool.memset(zero[:], 0.0).then_inc(always, 1)
            pool.memset(ones[:], 1.0).then_inc(consts, 1)
            pool.memset(zeros_e[:], 0.0).then_inc(consts, 1)
            pool.iota(tile_no_i[:], pattern=[[1, TILES]], base=0, channel_multiplier=0).then_inc(consts, 1)
            pool.iota(full_i[:], pattern=[[RT, NCMP]], base=0, channel_multiplier=0).then_inc(consts, 1)
            pool.iota(first_i[:], pattern=[[REGION, NE]], base=0, channel_multiplier=0).then_inc(consts, 1)
            pool.iota(spare_i[:], pattern=[[128, TILES * RB]], base=1 + SLOTS,
                      channel_multiplier=1).then_inc(consts, 1)
            pool.wait_ge(own, 1)
            pool.affine_select(out=ident[:], in_=ident[:], compare_op=ALU.not_equal, fill=1.0, base=0,
                               pattern=[[-1, 128]], channel_multiplier=1).then_inc(consts, 1)

            def lo_of(raw, hi, lo, hi_ready, split, t):
                wait(pool, hi_ready, t + 1)
                pool.tensor_tensor(lo[:], raw[:], hi[:].bitcast(F32), ALU.subtract).then_inc(split, 1)

            def turn(t, par, s):
                if on(t + 1):
                    lo_of(w1_raw[1 - par], w1_hi[1 - par], w1_lo[1 - par], w1_hi_ready, w1_split, t + 1)
                if on(t):
                    wait(pool, w2_hi_ready, t + 1)
                    pool.tensor_tensor(w2_lo[par][:, 0:FM - 1], w2_raw[par][:, 0:FM - 1],
                                       w2_hi[par][:, 0:FM - 1].bitcast(F32), ALU.subtract)
                if on(t - 1):
                    wait(pool, y_read, RB * t)
                if on(t):
                    pool.tensor_tensor(w2_lo[par][:, FM - 1], w2_raw[par][:, FM - 1],
                                       w2_hi[par][:, FM - 1].bitcast(F32), ALU.subtract).then_inc(w2_split, 1)
                if on(t - 1):
                    for r in range(RB):
                        pool.indirect_dma_start(
                            out=ys, out_offset=bass.IndirectOffsetOnAxis(ap=slot[1 - par][:, r:r + 1], axis=0),
                            in_=y_t[1 - par][:, r, :], in_offset=None).then_inc(y_stored[1 - par], 16)

            lo_of(w1_raw[0], w1_hi[0], w1_lo[0], w1_hi_ready, w1_split, 0)
            turns(pool, turn)
            for p in range(2):
                pool.wait_ge(y_stored[p], 16 * RB * ((TILES + 1 - p) // 2))

        @block.sync
        def _(sp):
            sp.wait_ge(table_ready, 1)
            sp.wait_ge(always, 1)
            for e in range(NE):
                row = sp.value_load(table[0:1, 3 * TILES + e:3 * TILES + e + 1], min_val=0,
                                    max_val=NE * REGION - RT)
                sp.dma_start(xs[bass.ds(row, RT), :].rearrange("(r p) d -> p r d", p=128),
                             zero[:]).then_inc(cleared, 16)
            sp.wait_ge(cleared, 16 * NE)

            def load(t, par):
                def ready(sem, value):
                    wait(sp, sem, value)
                    sp.wait_ge(always, 1)

                expert = sp.value_load(table[0:1, bass.ds(t, 1)], min_val=0, max_val=NE - 1)
                row = sp.value_load(table[0:1, bass.ds(t + TILES, 1)], min_val=0, max_val=NE * REGION - RT)
                ready(slot_ready, t - 1)
                sp.dma_start(x_t[par][:], xs[bass.ds(row, RT), :].rearrange("(r p) d -> p r d", p=128)
                             ).then_inc(x_in[par], 16)
                ready(w1_split, t - 1)
                sp.dma_start(w1_raw[par][:], w1[expert]).then_inc(w1_in[par], 16)
                ready(h_relu, FM * (t - 1))
                sp.dma_start(b1_c[par][:], b1[expert]).then_inc(b1_in[par], 16)
                ready(w2_split, t - 1)
                sp.dma_start(w2_raw[par][:], w2[expert]).then_inc(w2_in[par], 16)

            def turn(t, par, s):
                if on(t + 2):
                    load(t + 2, par)

            load(0, 0)
            load(1, 1)
            turns(sp, turn)

        @block.scalar
        def _(act):
            def load_b2(t, par):
                expert = act.value_load(table[0:1, bass.ds(t, 1)], min_val=0, max_val=NE - 1)
                act.dma_start(b2_b[par][:], b2[expert].partition_broadcast(128)).then_inc(b2_in[par], 16)

            def x_hi():
                act.activation(xT_hi[:].rearrange("p k t -> p (k t)"), xT_ps[:], ACT.Copy).then_inc(xT_hi_ready, 1)

            act.wait_ge(table_ready, 1)
            load_b2(0, 0)
            wait(act, xT_done, 1)
            x_hi()

            def turn(t, par, s):
                if on(t):
                    for c in range(FM):
                        wait(act, h_done, FM * t + c + 1)
                        if c == 0:
                            wait(act, b1_in[par], 16 * nth(s, par))
                            wait(act, h_split, FM * (t - 1))
                        act.activation(h_raw[par][:, c, :], h_ps[c][:, 0:RT], ACT.Relu,
                                       bias=b1_c[par][:, c:c + 1]).then_inc(h_relu, 1)
                if on(t + 1):
                    wait(act, xT_done, t + 2)
                    x_hi()
                if on(t + 1):
                    wait(act, b2_w_ready, t)
                    load_b2(t + 1, 1 - par)

            turns(act, turn)

        @block.vector
        def _(dve):
            n_own = [1]

            def link(ins):
                n_own[0] += 1
                ins.then_inc(own, 1)
                dve.wait_ge(own, n_own[0])

            def wide(ap, shape, axis):
                return ap.unsqueeze(axis).broadcast_to(shape)

            dve.wait_ge(own, 1)
            dve.wait_ge(consts, 7)
            link(dve.tensor_copy(tile_no[:], tile_no_i[:]))
            link(dve.tensor_copy(full[:], full_i[:]))
            link(dve.tensor_copy(first[:], first_i[:]))
            link(dve.tensor_copy(spare[:], spare_i[:]))
            dve.wait_ge(totals_done, 1)
            link(dve.tensor_copy(totals[:], y_ps[0][:, 0:2 * NE]))
            link(dve.tensor_scalar(tmp[:], totals[:, 0:NE], 1.0, None, ALU.max))
            link(dve.reciprocal(tmp[:], tmp[:]))
            link(dve.memset(wexp[:, NE:NE + 1], 0.0))
            link(dve.tensor_tensor(wexp[:, 0:NE], totals[:, NE:2 * NE], tmp[:], ALU.mult))
            link(dve.tensor_tensor(more[:], wide(totals[:, 0:NE], [128, NE, NCMP], 2),
                                   wide(full[:], [128, NE, NCMP], 1), ALU.is_gt))
            link(dve.tensor_reduce(ntiles[:], more[:], AX.X, ALU.add))
            link(dve.tensor_tensor_scan(ends[:], ntiles[:], zeros_e[:], 0.0, ALU.add, ALU.add))
            link(dve.tensor_tensor(past[:], wide(ends[:], [128, TILES, NE], 1),
                                   wide(tile_no[:], [128, TILES, NE], 2), ALU.is_le))
            link(dve.tensor_tensor(skipped[:], past[:], wide(ntiles[:], [128, TILES, NE], 1), ALU.mult))
            link(dve.tensor_reduce(t_exp[:], past[:], AX.X, ALU.add))
            link(dve.tensor_reduce(t_before[:], skipped[:], AX.X, ALU.add))
            link(dve.tensor_scalar(t_valid[:], t_exp[:], float(NE) - 0.5, float(RT), ALU.is_lt, ALU.mult))
            link(dve.tensor_copy(table[:, 2 * TILES:3 * TILES], t_exp[:]))
            link(dve.tensor_scalar(t_exp[:], t_exp[:], float(NE - 1), None, ALU.min))
            link(dve.tensor_tensor(t_row[:], tile_no[:], t_before[:], ALU.subtract))
            link(dve.tensor_tensor(t_row[:], t_row[:], t_valid[:], ALU.mult))
            link(dve.scalar_tensor_tensor(t_row[:], t_exp[:], float(REGION), t_row[:], ALU.mult, ALU.add))
            link(dve.tensor_tensor(pad[:], first[:], totals[:, 0:NE], ALU.add))
            link(dve.tensor_copy(table[:, 0:TILES], t_exp[:]))
            link(dve.tensor_copy(table[:, TILES:2 * TILES], t_row[:]))
            dve.tensor_copy(table[:, 3 * TILES:], pad[:]).then_inc(table_ready, 1)

            def hi_of(count, par, raw, hi, loaded, done, ready):
                wait(dve, loaded[par], 16 * count)
                done()
                dve.tensor_copy(hi[par][:], raw[par][:]).then_inc(ready, 1)

            def x_lo(t):
                wait(dve, xT_hi_ready, t + 1)
                dve.tensor_tensor(xT_lo[:].rearrange("p k t -> p (k t)"), xT_ps[:],
                                  xT_hi[:].bitcast(F32).rearrange("p k t -> p (k t)"),
                                  ALU.subtract).then_inc(xT_split, 1)

            hi_of(1, 0, w1_raw, w1_hi, w1_in, lambda: None, w1_hi_ready)
            x_lo(0)

            def turn(t, par, s):
                if on(t + 1):
                    hi_of(nth(s, par, 1), 1 - par, w1_raw, w1_hi, w1_in, lambda: wait(dve, h_done, FM * t), w1_hi_ready)
                if on(t):
                    hi_of(nth(s, par), par, w2_raw, w2_hi, w2_in, lambda: wait(dve, y_done, RB * (t - 1)), w2_hi_ready)
                    for c in range(FM):
                        wait(dve, h_relu, FM * t + c + 1)
                        dve.tensor_copy(h_hi[par][:, c, :], h_raw[par][:, c, :]).then_inc(h_hi_ready, 1)
                        wait(dve, h_hi_ready, FM * t + c + 1)
                        dve.tensor_tensor(h_lo[par][:, c, :], h_raw[par][:, c, :],
                                          h_hi[par][:, c, :].bitcast(F32), ALU.subtract).then_inc(h_split, 1)
                if on(t):
                    column = dve.value_load(table[0:1, bass.ds(t + 2 * TILES, 1)], min_val=0, max_val=NE)
                    wait(dve, x_in[par], 16 * nth(s, par))
                    of_rows = x_t[par][:, :, bass.ds(column + D, 1)].rearrange("p r o -> p (r o)")
                    dve.scalar_tensor_tensor(no_slot[:], of_rows, 0.0, spare[:, bass.ds(t * RB, RB)],
                                             ALU.is_equal, ALU.mult).then_inc(no_slot_ready, 1)
                    wait(dve, no_slot_ready, t + 1)
                    wait(dve, y_stored[par], 16 * RB * (nth(s, par) - 1))
                    dve.tensor_tensor(slot[par][:], no_slot[:], of_rows, ALU.add).then_inc(slot_ready, 1)
                if on(t + 1):
                    x_lo(t + 1)
                if on(t - 1):
                    expert = dve.value_load(table[0:1, bass.ds(t - 1 + 2 * TILES, 1)], min_val=0, max_val=NE)
                    weight = wexp[:, bass.ds(expert, 1)]
                    wait(dve, b2_in[1 - par], 16 * nth(s, par, -1))
                    wait(dve, y_read, RB * (t - 2))
                    dve.tensor_scalar(b2_w[1 - par][:], b2_b[1 - par][:], weight, None, ALU.mult).then_inc(b2_w_ready, 1)
                    wait(dve, b2_w_ready, t)
                    wait(dve, y_stored[1 - par], 16 * RB * (nth(s, par, -1) - 1))
                    for r in range(RB):
                        wait(dve, y_done, RB * (t - 1) + r + 1)
                        dve.scalar_tensor_tensor(y_t[1 - par][:, r, :], y_ps[r][:, 0:D], weight, b2_w[1 - par][:],
                                                 ALU.mult, ALU.add).then_inc(y_read, 1)

            turns(dve, turn)

        @block.tensor
        def _(pe):
            pe.wait_ge(consts, 7)
            pe.matmul(y_ps[0][:, 0:2 * NE], ones[:], counts[:], start=True, stop=True).then_inc(totals_done, 1)

            def transpose_x(t, par, count):
                wait(pe, x_in[par], 16 * count)
                wait(pe, xT_split, t)
                for k in range(KD):
                    for r in range(RB):
                        ins = pe.transpose(xT_ps[:, k * RT + 128 * r:k * RT + 128 * r + 128],
                                           x_t[par][:, r, 128 * k:128 * k + 128], ident[:])
                ins.then_inc(xT_done, 1)

            transpose_x(0, 0, 1)

            def turn(t, par, s):
                if on(t):
                    wait(pe, w1_split, t + 1)
                    wait(pe, xT_split, t + 1)
                    for c in range(FM):
                        wait(pe, h_relu, FM * (t - 1) + c + 1)
                        for k in range(KD):
                            for p, (w, a) in enumerate(((w1_hi, xT_hi), (w1_hi, xT_lo), (w1_lo, xT_hi))):
                                ins = pe.matmul(h_ps[c][:, 0:RT], w[par][:, k, 128 * c:128 * c + 128], a[:, k, :],
                                                start=(k == 0 and p == 0), stop=(k == KD - 1 and p == 2))
                        ins.then_inc(h_done, 1)
                if on(t + 1):
                    transpose_x(t + 1, 1 - par, nth(s, par, 1))
                if on(t - 1):
                    other = 1 - par
                    wait(pe, w2_split, t)
                    wait(pe, h_split, FM * t)
                    for r in range(RB):
                        wait(pe, y_read, RB * (t - 2) + r + 1)
                        rows = slice(128 * r, 128 * r + 128)
                        for m in range(FM):
                            for p, (h, w) in enumerate(((h_hi, w2_hi), (h_hi, w2_lo), (h_lo, w2_hi))):
                                ins = pe.matmul(y_ps[r][:, 0:D], h[other][:, m, rows], w[other][:, m, :],
                                                start=(m == 0 and p == 0), stop=(m == FM - 1 and p == 2))
                        ins.then_inc(y_done, 1)

            turns(pe, turn)


def combine(nc, ys, x1s, g_ffn, wp1, bp1, wp2, bp2, out):
    with ExitStack() as ctx:
        def sb(name, shape, dt=F32):
            return ctx.enter_context(nc.sbuf_tensor(name, shape, dt))

        def pb(name, shape):
            return ctx.enter_context(nc.psum_tensor(name, shape, F32))

        def sem(name):
            return ctx.enter_context(nc.semaphore(name))

        PART = 4
        x1 = sb("x1_all", [SQ, B, D])
        y = sb("y", [SQ, TOPK, B, D])
        mixed = y[:, 0]
        ones = sb("ones3", [SQ, SQ])
        wp1_sb = sb("wp1_sb", [128, KD, 128])
        bp1_c = sb("bp1_c", [128, 1])
        wp2_c = sb("wp2_c", [128, 1])
        bp2_c = sb("bp2_c", [1, 1])
        gate_raw = sb("gate2_raw", [128, 1])
        gate = sb("gate2", [128, 1])
        pooled = sb("pooled", [128, KD, B])
        hidden = sb("hidden", [128, B])
        phi = sb("phi", [1, 5, B])
        factor = sb("factor", [SQ, B])
        pool_ps = pb("pool_ps", [128, KD, B])
        mlp_ps = pb("mlp_ps", [128, 512])
        phi_ps = pb("phi_ps", [128, 512])
        factor_ps = pb("factor_ps", [128, 512])

        loaded = sem("loaded3")
        x1_in = sem("x1_in")
        y_in = [sem(f"y_in{i}") for i in range(B // PART)]
        consts = sem("consts3")
        own = sem("own3")
        two_added = sem("two_added")
        mixed_ready = sem("mixed_ready")
        pooled_done = sem("pooled_done")
        act_done = sem("act_done")
        pe_done = sem("pe_done3")
        phi_in = sem("phi_in")
        phi_ready = sem("phi_ready")
        final = sem("final")
        stored = sem("stored")
        slots = ys[1:1 + SLOTS, :].rearrange("(k b s) d -> k s b d", k=TOPK, b=B)

        block = ctx.enter_context(nc.Block())

        @block.sync
        def _(sp):
            for i in range(B // PART):
                part = slice(PART * i, PART * (i + 1))
                for k in range(TOPK):
                    sp.dma_start(y[:, k, part, :], slots[k, :, part, :]).then_inc(y_in[i], 16)
            sp.dma_start(wp1_sb[:], wp1).then_inc(loaded, 16)
            sp.dma_start(bp1_c[:], bp1).then_inc(loaded, 16)
            sp.dma_start(wp2_c[:], wp2).then_inc(loaded, 16)
            sp.dma_start(bp2_c[:], bp2.partition_broadcast(1)).then_inc(loaded, 16)
            sp.dma_start(gate_raw[:], g_ffn.partition_broadcast(128)).then_inc(loaded, 16)
            sp.dma_start(x1[:], x1s.rearrange("b s d -> s b d")).then_inc(x1_in, 16)
            for i in range(B // PART):
                sp.wait_ge(final, PART * (i + 1))
                part = slice(PART * i, PART * (i + 1))
                sp.dma_start(out[part].rearrange("b s d -> s b d"), x1[:, part, :]).then_inc(stored, 16)
            sp.wait_ge(stored, 16 * B // PART)

        @block.gpsimd
        def _(pool):
            pool.memset(ones[:], 1.0).then_inc(consts, 1)

        @block.vector
        def _(dve):
            n_own = [0]

            def link(ins):
                n_own[0] += 1
                ins.then_inc(own, 1)
                dve.wait_ge(own, n_own[0])

            for i in range(B // PART):
                part = slice(PART * i, PART * (i + 1))
                dve.wait_ge(y_in[i], 16 * TOPK)
                dve.tensor_tensor(mixed[:, part], y[:, 0, part], y[:, 1, part], ALU.add).then_inc(two_added, 1)
                dve.wait_ge(two_added, i + 1)
                dve.tensor_tensor(mixed[:, part], mixed[:, part], y[:, 2, part], ALU.add).then_inc(mixed_ready, 1)
            dve.wait_ge(act_done, 4)
            link(dve.tensor_scalar(phi[:, 1, :], phi[:, 0, :], 1.0, None, ALU.add))
            link(dve.reciprocal(phi[:, 2, :], phi[:, 1, :]))
            link(dve.tensor_scalar(phi[:, 3, :], phi[:, 2, :], 0.7, None, ALU.is_gt))
            dve.tensor_scalar(phi[:, 4, :], phi[:, 3, :], -0.8, 1.0, ALU.mult, ALU.add).then_inc(phi_ready, 1)
            dve.wait_ge(pe_done, 3)
            link(dve.tensor_scalar(factor[:], factor_ps[0:SQ, 0:B], gate[0:SQ], None, ALU.mult))
            dve.wait_ge(x1_in, 16)
            for b in range(B):
                dve.scalar_tensor_tensor(x1[:, b, :], mixed[:, b, :], factor[:, b:b + 1], x1[:, b, :],
                                         ALU.mult, ALU.add).then_inc(final, 1)

        @block.tensor
        def _(pe):
            pe.wait_ge(consts, 1)
            pe.wait_ge(loaded, 16 * 5)
            for b in range(B):
                pe.wait_ge(mixed_ready, b // PART + 1)
                for k in range(KD):
                    last = pe.matmul(pool_ps[:, k, b:b + 1], mixed[:, b, 128 * k:128 * k + 128], ones[:, 0:1],
                                     start=True, stop=True)
            last.then_inc(pooled_done, 1)
            pe.wait_ge(act_done, 2)
            for k in range(KD):
                last = pe.matmul(mlp_ps[:, 0:B], wp1_sb[:, k, :], pooled[:, k, :], start=(k == 0), stop=(k == KD - 1))
            last.then_inc(pe_done, 1)
            pe.wait_ge(act_done, 3)
            pe.matmul(phi_ps[0:1, 0:B], wp2_c[:], hidden[:], start=True, stop=True).then_inc(pe_done, 1)
            pe.wait_ge(phi_ready, 1)
            pe.matmul(factor_ps[0:SQ, 0:B], ones[0:1, :], phi[:, 4, :], start=True, stop=True).then_inc(pe_done, 1)

        @block.scalar
        def _(act):
            act.wait_ge(loaded, 16 * 5)
            act.activation(gate[:], gate_raw[:], ACT.Tanh).then_inc(act_done, 1)
            act.wait_ge(pooled_done, 1)
            act.activation(pooled[:], pool_ps[:], ACT.Copy, scale=1.0 / SQ).then_inc(act_done, 1)
            act.wait_ge(pe_done, 1)
            act.activation(hidden[:], mlp_ps[:, 0:B], ACT.Relu, bias=bp1_c[:]).then_inc(act_done, 1)
            act.wait_ge(pe_done, 2)
            act.activation(phi[:, 3, :], phi_ps[0:1, 0:B], ACT.Identity, bias=bp2_c[:]).then_inc(phi_in, 1)
            act.wait_ge(phi_in, 1)
            act.activation(phi[:, 0, :], phi[:, 3, :], ACT.Exp, scale=-1.0).then_inc(act_done, 1)


def kernel(**inputs):
    import numpy as np
    import concourse.bacc as bacc
    from concourse.bass_utils import run_bass_kernel_spmd

    def halves(a):
        return a.reshape(-1, 128, a.shape[-1]).transpose(1, 0, 2)

    a = {k: np.asarray(v) for k, v in inputs.items()}
    xa, ff = "L0_xattn_", "L0_ffn_"
    arrays = {
        "x": a["x"],
        "ctxT": a["ctx_2048"].reshape(B, T, KD, 128).transpose(0, 3, 2, 1),
        "g_xattn": a["g_xattn"],
        "g_ffn": a["g_ffn"],
        "wqT": halves(a[xa + "Wq"].T), "bq": a[xa + "bq"].reshape(KD, 128).T,
        "wkT": halves(a[xa + "Wk"].T), "bk": a[xa + "bk"].reshape(KD, 128).T,
        "wvT": halves(a[xa + "Wv"].T), "bv": a[xa + "bv"].reshape(KD, 128).T,
        "woT": halves(a[xa + "Wo"].T), "bo": a[xa + "bo"],
        "wr": halves(a[ff + "Wr"]), "br": a[ff + "br"],
        "w1": a[ff + "w1"].reshape(NE, KD, 128, FF).transpose(0, 2, 1, 3),
        "b1": a[ff + "b1"].reshape(NE, FM, 128).transpose(0, 2, 1),
        "w2": a[ff + "w2"].reshape(NE, FM, 128, D).transpose(0, 2, 1, 3), "b2": a[ff + "b2"],
        "wp1": halves(a[ff + "Wp1"]), "bp1": a[ff + "bp1"].reshape(128, 1),
        "wp2": a[ff + "Wp2"], "bp2": a[ff + "bp2"],
    }
    arrays = {f"in_{k}": np.ascontiguousarray(v) for k, v in arrays.items()}
    nc = bacc.Bacc("TRN2", target_bir_lowering=False, num_devices=1)
    args = [nc.dram_tensor(k, v.shape, F32, kind="ExternalInput").ap() for k, v in arrays.items()]
    names = [k[3:] for k in arrays]
    out = nc.dram_tensor("out", [B, SQ, D], F32, kind="ExternalOutput").ap()
    program(nc, out=out, **dict(zip(names, args)))
    r = run_bass_kernel_spmd(nc, [arrays], core_ids=[0])
    return r.results[0]["out"]
```
